# Optimizing a Trainium2 kernel written in Bass

```python
import numpy as np
import jax
import jax.numpy as jnp

def _softmax(x, axis=-1):
    return jax.nn.softmax(x, axis=axis)

def _gelu(x):
    return jax.nn.gelu(x, approximate=True)

def _silu(x):
    return jax.nn.silu(x)

def _sigmoid(x):
    return jax.nn.sigmoid(x)

def _layernorm(x, axis=-1, eps=1e-05):
    m = jnp.mean(x, axis=axis, keepdims=True)
    v = jnp.var(x, axis=axis, keepdims=True)
    return (x - m) / jnp.sqrt(v + eps)

def _scatter_add(tgt, idx, src, axis=0):
    return tgt.at[idx].add(src)

def _segment_sum(src, seg, n):
    return jax.ops.segment_sum(src, seg, n)
kernel_name = 'mk_conv_seq_d2_conv_nchw16_r2_a29974'

def setup_inputs(seed: int=0):
    np.random.seed(seed)
    _w = jnp.asarray

    def _rec_inputs():
        import jax
        import jax.numpy as jnp
        _gk = jax.random.key(seed)
        x = -7.109e-05 + 0.9999 * jax.random.normal(jax.random.fold_in(_gk, 1), (1, 16, 1024, 1024), jnp.float32)
        return x
    x = _rec_inputs()

    def _L0_conv_setup():
        import jax, jax.numpy as jnp
        import numpy as np
        B, H, T, S = (1, 16, 1024, 1024)
        G, I = (1, 2)
        M = H // G
        key = jax.random.key(seed)
        ks = jax.random.split(key, 8)
        scale = 0.02
        return {'inputs': jax.random.normal(ks[0], (B, H, T, S), dtype=jnp.float32), 'w': jax.random.normal(ks[1], (G, M, M), dtype=jnp.float32) * scale, 'qw1': jax.random.normal(ks[2], (B, T, G, I, M), dtype=jnp.float32) * scale, 'qw2': jax.random.normal(ks[3], (B, T, G, I, M), dtype=jnp.float32) * scale, 'kw1': jax.random.normal(ks[4], (B, S, G, I, M), dtype=jnp.float32) * scale, 'kw2': jax.random.normal(ks[5], (B, S, G, I, M), dtype=jnp.float32) * scale, 'qdd': jax.random.normal(ks[6], (B, T, G, M), dtype=jnp.float32) * scale, 'kdd': jax.random.normal(ks[7], (B, S, G, M), dtype=jnp.float32) * scale}
    _L0_conv_all = _L0_conv_setup()
    _L0_conv_in = {k: v for k, v in _L0_conv_all.items() if k in ('w', 'qw1', 'qw2', 'kw1', 'kw2', 'qdd', 'kdd')}
    del _L0_conv_all

    def _L1_conv_setup():
        import jax, jax.numpy as jnp
        import numpy as np
        B, H, T, S = (1, 16, 1024, 1024)
        G, I = (1, 2)
        M = H // G
        key = jax.random.key(seed)
        ks = jax.random.split(key, 8)
        scale = 0.02
        return {'inputs': jax.random.normal(ks[0], (B, H, T, S), dtype=jnp.float32), 'w': jax.random.normal(ks[1], (G, M, M), dtype=jnp.float32) * scale, 'qw1': jax.random.normal(ks[2], (B, T, G, I, M), dtype=jnp.float32) * scale, 'qw2': jax.random.normal(ks[3], (B, T, G, I, M), dtype=jnp.float32) * scale, 'kw1': jax.random.normal(ks[4], (B, S, G, I, M), dtype=jnp.float32) * scale, 'kw2': jax.random.normal(ks[5], (B, S, G, I, M), dtype=jnp.float32) * scale, 'qdd': jax.random.normal(ks[6], (B, T, G, M), dtype=jnp.float32) * scale, 'kdd': jax.random.normal(ks[7], (B, S, G, M), dtype=jnp.float32) * scale}
    _L1_conv_all = _L1_conv_setup()
    _L1_conv_in = {k: v for k, v in _L1_conv_all.items() if k in ('w', 'qw1', 'qw2', 'kw1', 'kw2', 'qdd', 'kdd')}
    del _L1_conv_all
    return {'x': x, 'L0_conv_w': _L0_conv_in['w'], 'L0_conv_qw1': _L0_conv_in['qw1'], 'L0_conv_qw2': _L0_conv_in['qw2'], 'L0_conv_kw1': _L0_conv_in['kw1'], 'L0_conv_kw2': _L0_conv_in['kw2'], 'L0_conv_qdd': _L0_conv_in['qdd'], 'L0_conv_kdd': _L0_conv_in['kdd'], 'L1_conv_w': _L1_conv_in['w'], 'L1_conv_qw1': _L1_conv_in['qw1'], 'L1_conv_qw2': _L1_conv_in['qw2'], 'L1_conv_kw1': _L1_conv_in['kw1'], 'L1_conv_kw2': _L1_conv_in['kw2'], 'L1_conv_qdd': _L1_conv_in['qdd'], 'L1_conv_kdd': _L1_conv_in['kdd']}

def reference(x, L0_conv_w, L0_conv_qw1, L0_conv_qw2, L0_conv_kw1, L0_conv_kw2, L0_conv_qdd, L0_conv_kdd, L1_conv_w, L1_conv_qw1, L1_conv_qw2, L1_conv_kw1, L1_conv_kw2, L1_conv_qdd, L1_conv_kdd):
    import jax
    import jax.numpy as jnp

    def _L0_conv_ref(inputs, w, qw1, qw2, kw1, kw2, qdd, kdd):
        import jax, jax.numpy as jnp
        import numpy as np
        B, H, T, S = (1, 16, 1024, 1024)
        G, I = (1, 2)
        M = H // G
        b, h, t, s = inputs.shape
        x = inputs.reshape(b, G, h // G, t, s)
        wI = w + jnp.eye(w.shape[-1], dtype=w.dtype)
        ret = jnp.einsum('BGMTS,GMN->BGNTS', x, wI)
        hq = jnp.einsum('BGMTS,BTGIM->BGITS', x, qw1)
        ret = ret + jnp.einsum('BGITS,BTGIM->BGMTS', hq, qw2)
        hk = jnp.einsum('BGMTS,BSGIM->BGITS', x, kw1)
        ret = ret + jnp.einsum('BGITS,BSGIM->BGMTS', hk, kw2)
        ret = ret + x * qdd.transpose(0, 2, 3, 1)[:, :, :, :, None]
        ret = ret + x * kdd.transpose(0, 2, 3, 1)[:, :, :, None, :]
        return ret.reshape(b, h, t, s)

    def _L1_conv_ref(inputs, w, qw1, qw2, kw1, kw2, qdd, kdd):
        import jax, jax.numpy as jnp
        import numpy as np
        B, H, T, S = (1, 16, 1024, 1024)
        G, I = (1, 2)
        M = H // G
        b, h, t, s = inputs.shape
        x = inputs.reshape(b, G, h // G, t, s)
        wI = w + jnp.eye(w.shape[-1], dtype=w.dtype)
        ret = jnp.einsum('BGMTS,GMN->BGNTS', x, wI)
        hq = jnp.einsum('BGMTS,BTGIM->BGITS', x, qw1)
        ret = ret + jnp.einsum('BGITS,BTGIM->BGMTS', hq, qw2)
        hk = jnp.einsum('BGMTS,BSGIM->BGITS', x, kw1)
        ret = ret + jnp.einsum('BGITS,BSGIM->BGMTS', hk, kw2)
        ret = ret + x * qdd.transpose(0, 2, 3, 1)[:, :, :, :, None]
        ret = ret + x * kdd.transpose(0, 2, 3, 1)[:, :, :, None, :]
        return ret.reshape(b, h, t, s)

    def _gn(v, G=8, eps=1e-05):
        B_, C_, H_, W_ = v.shape
        g = v.reshape(B_, G, C_ // G, H_, W_)
        m = jnp.mean(g, axis=(2, 3, 4), keepdims=True)
        s = jnp.var(g, axis=(2, 3, 4), keepdims=True)
        return ((g - m) / jnp.sqrt(s + eps)).reshape(v.shape)

    def _ln_c(v, eps=1e-06):
        m = jnp.mean(v, axis=1, keepdims=True)
        s = jnp.var(v, axis=1, keepdims=True)
        return (v - m) / jnp.sqrt(s + eps)

    def _ln_t(v, eps=1e-05):
        m = jnp.mean(v, axis=-1, keepdims=True)
        s = jnp.var(v, axis=-1, keepdims=True)
        return (v - m) / jnp.sqrt(s + eps)

    def _to_tokens(v):
        B_, C_, H_, W_ = v.shape
        return v.reshape(B_, C_, H_ * W_).transpose(0, 2, 1)

    def _from_tokens(t, like):
        B_, C_, H_, W_ = like.shape
        return t.transpose(0, 2, 1).reshape(B_, C_, H_, W_)
    x = _L0_conv_ref(x, L0_conv_w, L0_conv_qw1, L0_conv_qw2, L0_conv_kw1, L0_conv_kw2, L0_conv_qdd, L0_conv_kdd)
    x = _L1_conv_ref(x, L1_conv_w, L1_conv_qw1, L1_conv_qw2, L1_conv_kw1, L1_conv_kw2, L1_conv_qdd, L1_conv_kdd)
    return x

_drawn_inputs = setup_inputs


def setup_inputs(seed=0):
    import zlib

    import numpy as np

    out = dict(_drawn_inputs(seed))
    spreads = {}
    factors = {'L0_conv_qw1': 8.0,
     'L0_conv_qw2': 8.0,
     'L0_conv_kw1': 8.0,
     'L0_conv_kw2': 8.0,
     'L0_conv_qdd': 2.851,
     'L0_conv_kdd': 2.847,
     'L1_conv_qw1': 8.0,
     'L1_conv_qw2': 8.0,
     'L1_conv_kw1': 8.0,
     'L1_conv_kw2': 8.0,
     'L1_conv_qdd': 2.851,
     'L1_conv_kdd': 2.847}
    for name, (base, spread) in spreads.items():
        noise = np.random.default_rng([zlib.crc32(name.encode()), seed]).standard_normal(out[name].shape)
        drawn = base * np.exp(spread * noise) if base else spread * noise
        out[name] = jnp.asarray(drawn.astype(out[name].dtype))
    for name, factor in factors.items():
        out[name] = (out[name] * factor).astype(out[name].dtype)
    return out
```

```python
import concourse.bass as bass
from concourse import mybir
from contextlib import ExitStack

P = 128
CH = 16
SPLIT = P // CH
T, S = 1024, 1024
COLS = S // SPLIT
ROWS = 128
BLOCKS = T // ROWS
RANK = 2
LAYERS = 2
GRP = 4
GROUPS = ROWS // GRP
RING = 4
AHEAD = 3
LAG = 2
CHUNK = 32
CHUNKS = ROWS // CHUNK
CGROUPS = CHUNK // GRP
PARAMS = 2 * RANK * CH + CH
DMA = 16
ATURN = 4
TBANKS = CH // GRP


def cross_conv_kernel(nc, x, row_params, col_params, w, out):
    f32 = mybir.dt.float32
    ALU = mybir.AluOpType
    ACT = mybir.ActivationFunctionType

    ctx = ExitStack()
    with ctx:
        def sb(name, shape):
            return ctx.enter_context(nc.sbuf_tensor(name, shape, f32))

        def sem(name):
            return ctx.enter_context(nc.semaphore(name))

        X = sb("X", [P, ROWS, COLS])
        Y = sb("Y", [P, ROWS, COLS])
        OUT = sb("OUT", [P, 2, CHUNK, COLS])
        RT = [sb(f"RT{l}", [P, ROWS, CH]) for l in range(LAYERS)]
        RS = [sb(f"RS{l}", [P, COLS, CH]) for l in range(LAYERS)]
        WA = sb("WA", [P, RING, GRP, SPLIT, CH])
        WB = sb("WB", [P, RING, GRP, SPLIT, CH])
        ident = sb("ident", [P, P])
        mask = sb("mask", [P, SPLIT])
        PROD = sb("PROD", [P, RANK, CH, CH])
        QP = sb("QP", [P, LAYERS, PARAMS])
        scratch = OUT[:, :, :, :].rearrange("p a b c -> p (a b c)")
        area = SPLIT * CH * CH

        def part(start, size):
            return scratch[:, start:start + size]

        AT = [part(l * area, area).rearrange("t (p c n) -> t p c n", p=SPLIT, c=CH) for l in range(LAYERS)]
        AS = [part((1 + l) * area, area).rearrange("s (p c n) -> s p c n", p=SPLIT, c=CH) for l in range(LAYERS)]
        ASTMP = WB[:, :, :, :, :].rearrange("s r j p c -> s (r j p c)").rearrange(
            "s (p c n) -> s p c n", p=SPLIT, c=CH)
        KP = [part((1 + LAYERS) * area + l * SPLIT * PARAMS, SPLIT * PARAMS).rearrange("s (p v) -> s p v", p=SPLIT)
              for l in range(LAYERS)]
        WI = [part((1 + LAYERS) * area + LAYERS * SPLIT * PARAMS + l * CH * CH, CH * CH)
              .rearrange("s (c n) -> s c n", c=CH) for l in range(LAYERS)]

        PA = [ctx.enter_context(nc.psum_tensor(f"PA{i}", [P, GRP, P], f32)) for i in range(RING)]
        PB = [ctx.enter_context(nc.psum_tensor(f"PB{i}", [P, GRP, P], f32)) for i in range(RING)]

        x_loaded = [sem(f"x_loaded{j}") for j in range(CHUNKS)]
        q_loaded = sem("q_loaded")
        k_loaded = sem("k_loaded")
        consts_ready = sem("consts_ready")
        pool_step = sem("pool_step")
        dve_step = sem("dve_step")
        at_step = sem("at_step")
        at_ready = sem("at_ready")
        as_ready = sem("as_ready")
        r_full = sem("r_full")
        r_done = sem("r_done")
        wa_ready = sem("wa_ready")
        wb_ready = sem("wb_ready")
        a_full = sem("a_full")
        a_done = sem("a_done")
        b_full = sem("b_full")
        b_done = sem("b_done")
        stored = [sem(f"stored{b}") for b in range(2)]

        def before_t1(k):
            return 2 * GROUPS * k

        def before_s2(k):
            return 2 * GROUPS * k + GROUPS

        def before_s1(k):
            return 2 * GROUPS * k

        def before_t2(k):
            return 2 * GROUPS * k + GROUPS

        def before_r(k):
            return TBANKS + LAYERS * TBANKS + LAYERS * TBANKS * k

        def first(k):
            return isinstance(k, int) and k == 0

        def columns(buf, s):
            return buf[:, :, :].rearrange("p t s -> p s t")[:, bass.ds(s, GRP), :]

        def rows(buf, t):
            return buf[:, bass.ds(t, GRP), :]

        def spread(engine, dst, compact, at, ready):
            r = compact[:, bass.ds(at, GRP), :].unsqueeze(2).broadcast_to([P, GRP, SPLIT, CH])
            m = mask[:, :].unsqueeze(1).unsqueeze(3).broadcast_to([P, GRP, SPLIT, CH])
            engine.tensor_tensor(dst, r, m, ALU.mult).then_inc(ready, 1)

        block = ctx.enter_context(nc.Block())

        @block.sync
        def _(sp):
            def load_rows(l, k):
                w1, w2, dd = row_params[l]
                for src, at, size in ((w1, 0, RANK * CH), (w2, RANK * CH, RANK * CH), (dd, 2 * RANK * CH, CH)):
                    sp.dma_start(QP[:, l, at:at + size], src[bass.ds(k * ROWS, ROWS), :]).then_inc(q_loaded, DMA)

            def load_x(k, j):
                for p in range(SPLIT):
                    sp.dma_start(X[CH * p:CH * (p + 1), CHUNK * j:CHUNK * (j + 1), :],
                                 x[:, bass.ds(k * ROWS + CHUNK * j, CHUNK), COLS * p:COLS * (p + 1)]
                                 ).then_inc(x_loaded[j], DMA)

            def store(k, j):
                sp.wait_ge(b_done, before_t2(k) + CGROUPS * (j + 1))
                for p in range(SPLIT):
                    sp.dma_start(out[:, bass.ds(k * ROWS + CHUNK * j, CHUNK), COLS * p:COLS * (p + 1)],
                                 OUT[CH * p:CH * (p + 1), j % 2, :, :]).then_inc(stored[j % 2], DMA)

            load_rows(0, 0)
            for j in range(CHUNKS):
                load_x(0, j)
            sp.wait_ge(at_ready, 1)
            load_rows(1, 0)
            load_rows(0, 1)
            with sp.Fori(0, BLOCKS - 1) as k:
                for j in range(CHUNKS):
                    store(k, j)
                    load_x(k + 1, j)
                sp.wait_ge(at_ready, 1 + LAYERS * (k + 1))
                load_rows(1, k + 1)
                load_rows(0, (k + 2) % BLOCKS)
            for j in range(CHUNKS):
                store(BLOCKS - 1, j)
            for b in range(2):
                sp.wait_ge(stored[b], DMA * SPLIT * BLOCKS * CHUNKS // 2)

        @block.gpsimd
        def _(pool):
            nc.gpsimd.memset(ident[:, :], 0.0).then_inc(pool_step, 1)
            nc.gpsimd.memset(mask[:, :], 1.0).then_inc(pool_step, 1)
            pool.wait_ge(pool_step, 2)
            nc.gpsimd.affine_select(out=ident[:, :], in_=ident[:, :], compare_op=ALU.not_equal, fill=1.0,
                                    base=0, pattern=[[-1, P]], channel_multiplier=1).then_inc(consts_ready, 1)
            nc.gpsimd.affine_select(out=mask[:, :], in_=mask[:, :], compare_op=ALU.is_ge, fill=0.0,
                                    base=0, pattern=[[-CH, SPLIT]], channel_multiplier=1).then_inc(pool_step, 1)
            pool.wait_ge(pool_step, 3)
            nc.gpsimd.affine_select(out=mask[:, :], in_=mask[:, :], compare_op=ALU.is_ge, fill=0.0,
                                    base=CH - 1, pattern=[[CH, SPLIT]], channel_multiplier=-1
                                    ).then_inc(consts_ready, 1)
            pool.wait_ge(consts_ready, 2)

            def row_matrices(l, before):
                shape = [P, CH, CH]
                q1, q2 = ([QP[:, l, (RANK * j + i) * CH:(RANK * j + i + 1) * CH] for i in range(RANK)]
                          for j in range(2))
                for i in range(RANK):
                    nc.gpsimd.tensor_tensor(PROD[:, i], q1[i].unsqueeze(2).broadcast_to(shape),
                                            q2[i].unsqueeze(1).broadcast_to(shape), ALU.mult).then_inc(at_step, 1)
                pool.wait_ge(at_step, before + RANK)
                diagonal = PROD[:, 0].rearrange("t c n -> t (c n)")[:, 0:CH * CH:CH + 1]
                nc.gpsimd.tensor_tensor(diagonal, diagonal, QP[:, l, 2 * RANK * CH:PARAMS], ALU.add
                                        ).then_inc(at_step, 1)
                pool.wait_ge(at_step, before + RANK + 1)
                wide = [P, SPLIT, CH * CH]
                flat = [PROD[:, i].rearrange("t c n -> t (c n)").unsqueeze(1).broadcast_to(wide) for i in range(RANK)]
                nc.gpsimd.tensor_tensor(AT[l].rearrange("t p c n -> t p (c n)"), flat[0], flat[1], ALU.add
                                        ).then_inc(at_ready, 1)

            def both_row_matrices(k):
                steps = RANK + 1
                pool.wait_ge(q_loaded, DMA * 3 * (1 + LAYERS) + DMA * 3 * LAYERS * k)
                if first(k):
                    pool.wait_ge(r_full, before_r(0))
                else:
                    for b in range(2):
                        pool.wait_ge(stored[b], DMA * SPLIT * (CHUNKS // 2) * k)
                for n, l in enumerate((1, 0)):
                    pool.wait_ge(at_ready, 1 + n + LAYERS * k)
                    row_matrices(l, steps * (1 + n) + steps * LAYERS * k)

            pool.wait_ge(q_loaded, DMA * 3)
            row_matrices(0, 0)

            pool.wait_ge(r_done, TBANKS)
            for i in range(RING):
                spread(nc.gpsimd, WA[:, i], RT[0], GRP * i, wa_ready)
            with pool.Fori(1, GROUPS // RING) as it:
                for i in range(RING):
                    pool.wait_ge(a_full, RING * it + i - RING + 1)
                    spread(nc.gpsimd, WA[:, i], RT[0], GRP * (RING * it + i), wa_ready)

            def phase(compact, before, start, end, copied):
                with pool.Fori(start, end) as it:
                    pool.wait_ge(r_done, copied)
                    for i in range(RING):
                        pool.wait_ge(a_full, before + RING * it + i - RING + 1)
                        spread(nc.gpsimd, WA[:, i], compact, GRP * (RING * it + i), wa_ready)

            def s2_weights(k):
                phase(RS[1], before_s2(k), 0, ATURN, before_r(k))
                both_row_matrices(k)
                phase(RS[1], before_s2(k), ATURN, GROUPS // RING, before_r(k))

            def t1_weights(k):
                phase(RT[0], before_t1(k), 0, GROUPS // RING, before_r(k))

            s2_weights(0)
            t1_weights(1)
            with pool.Fori(1, BLOCKS - 1) as k:
                s2_weights(k)
                t1_weights(k + 1)
            s2_weights(BLOCKS - 1)

        @block.scalar
        def _(act):
            for l in range(LAYERS):
                w1, w2, dd = col_params[l]
                for src, at, size in ((w1, 0, RANK * CH), (w2, RANK * CH, RANK * CH), (dd, 2 * RANK * CH, CH)):
                    act.dma_start(KP[l][:, :, at:at + size], src.rearrange("(p s) v -> s p v", p=SPLIT)
                                  ).then_inc(k_loaded, DMA)
                act.dma_start(WI[l], w[l].unsqueeze(0).broadcast_to([P, CH, CH])).then_inc(k_loaded, DMA)

            def copy_compact(dst, before):
                for i in range(TBANKS):
                    act.wait_ge(r_full, before + i + 1)
                    nc.scalar.activation(dst[:, :, :].rearrange("p t n -> p n t")[:, GRP * i:GRP * (i + 1), :],
                                         PA[i][:, :, :], ACT.Copy).then_inc(r_done, 1)

            def copy_groups(dst, before):
                with act.Fori(0, GROUPS // RING) as it:
                    for i in range(RING):
                        act.wait_ge(a_full, before + RING * it + i + 1)
                        nc.scalar.activation(dst(GRP * (RING * it + i)), PA[i][:, :, :], ACT.Copy
                                             ).then_inc(a_done, 1)

            copy_compact(RT[0], 0)
            copy_groups(lambda at: rows(Y, at), before_t1(0))
            for l in range(LAYERS):
                copy_compact(RS[l], TBANKS * (1 + l))

            def s_phase(k):
                def copy(i, g):
                    act.wait_ge(a_full, before_s2(k) + g + 1)
                    nc.scalar.activation(columns(X, GRP * g), PA[i][:, :, :], ACT.Copy).then_inc(a_done, 1)

                turns = (GROUPS - RING - LAG) // RING
                with act.Fori(0, turns) as it:
                    for i in range(RING):
                        copy(i, RING * it + i)
                for g in range(RING * turns, GROUPS - RING - LAG):
                    copy(g % RING, g)
                act.wait_ge(wa_ready, before_s2(k))
                if not first(k):
                    act.wait_ge(wb_ready, before_s1(k))
                copy_compact(RT[1], before_r(k))
                copy_compact(RT[0], before_r(k) + TBANKS)
                for g in range(GROUPS - RING - LAG, GROUPS):
                    copy(g % RING, g)

            def block_steps(k):
                s_phase(k)
                copy_groups(lambda at: rows(Y, at), before_t1(k + 1))

            block_steps(0)
            with act.Fori(1, BLOCKS - 1) as k:
                block_steps(k)
            s_phase(BLOCKS - 1)

        @block.vector
        def _(dve):
            step = [0]

            def chained(instruction):
                step[0] += 1
                instruction.then_inc(dve_step, 1)
                dve.wait_ge(dve_step, step[0])

            def column_matrices(l):
                shape = [P, SPLIT, CH, CH]
                kw = [[KP[l][:, :, (RANK * j + i) * CH:(RANK * j + i + 1) * CH] for i in range(RANK)]
                      for j in range(2)]
                dd = KP[l][:, :, 2 * RANK * CH:PARAMS]
                for i in range(RANK):
                    chained(nc.vector.tensor_tensor((AS[l], ASTMP)[i], kw[0][i].unsqueeze(3).broadcast_to(shape),
                                                    kw[1][i].unsqueeze(2).broadcast_to(shape), ALU.mult))
                chained(nc.vector.tensor_tensor(AS[l], AS[l], ASTMP, ALU.add))
                diagonal = AS[l].rearrange("s p c n -> s p (c n)")[:, :, 0:CH * CH:CH + 1]
                chained(nc.vector.tensor_tensor(diagonal, diagonal, dd, ALU.add))
                wi = WI[l].rearrange("s c n -> s (c n)")
                chained(nc.vector.tensor_scalar(wi[:, 0:CH * CH:CH + 1], wi[:, 0:CH * CH:CH + 1], 1.0, None,
                                                ALU.add))
                nc.vector.tensor_tensor(AS[l], AS[l], WI[l].unsqueeze(1).broadcast_to(shape), ALU.add
                                        ).then_inc(as_ready, 1)

            def add_columns(i, k, g):
                dve.wait_ge(b_full, before_s1(k) + g + 1)
                at = columns(Y, GRP * g)
                nc.vector.tensor_tensor(at, PB[i][:, :, :], at, ALU.add).then_inc(b_done, 1)

            def add_rows(i, k, j, g):
                dve.wait_ge(b_full, before_t2(k) + CGROUPS * j + g + 1)
                nc.vector.tensor_tensor(OUT[:, j % 2, bass.ds(GRP * g, GRP), :], PB[i][:, :, :],
                                        rows(X, CHUNK * j + GRP * g), ALU.add).then_inc(b_done, 1)

            def s_phase(k):
                with dve.Fori(0, GROUPS // RING - 1) as it:
                    dve.wait_ge(a_done, before_s2(k))
                    for i in range(RING):
                        spread(nc.vector, WB[:, (i + AHEAD) % RING], RS[0], GRP * (RING * it + i + AHEAD), wb_ready)
                        add_columns(i, k, RING * it + i)
                for i in range(RING):
                    g = GROUPS - RING + i + AHEAD
                    if g == GROUPS:
                        dve.wait_ge(r_done, before_r(k) + TBANKS)
                    compact, g = (RS[0], g) if g < GROUPS else (RT[1], g - GROUPS)
                    spread(nc.vector, WB[:, (i + AHEAD) % RING], compact, GRP * g, wb_ready)
                    add_columns(i, k, GROUPS - RING + i)

            def t_phase(k, last):
                for j in range(CHUNKS):
                    whole = CGROUPS // RING - (j == CHUNKS - 1)
                    with dve.Fori(0, whole) as it:
                        dve.wait_ge(a_done, before_t1(k + 1))
                        dve.wait_ge(r_full, before_r(k + 1))
                        if j >= 2 or not first(k):
                            dve.wait_ge(stored[j % 2], DMA * SPLIT * (CHUNKS // 2 * k + j // 2))
                        for i in range(RING):
                            spread(nc.vector, WB[:, (i + AHEAD) % RING], RT[1],
                                   CHUNK * j + GRP * (RING * it + i + AHEAD), wb_ready)
                            add_rows(i, k, j, RING * it + i)
                for i in range(RING):
                    g = GROUPS - RING + i + AHEAD
                    if g < GROUPS:
                        spread(nc.vector, WB[:, (i + AHEAD) % RING], RT[1], GRP * g, wb_ready)
                    elif not last:
                        spread(nc.vector, WB[:, (i + AHEAD) % RING], RS[0], GRP * (g - GROUPS), wb_ready)
                    add_rows(i, k, CHUNKS - 1, CGROUPS - RING + i)

            dve.wait_ge(k_loaded, DMA * 4 * LAYERS)
            for l in range(LAYERS):
                column_matrices(l)
                dve.wait_ge(as_ready, l + 1)
            dve.wait_ge(consts_ready, 2)
            dve.wait_ge(r_done, 2 * TBANKS)
            for i in range(AHEAD):
                spread(nc.vector, WB[:, i], RS[0], GRP * i, wb_ready)
            s_phase(0)
            t_phase(0, False)
            with dve.Fori(1, BLOCKS - 1) as k:
                s_phase(k)
                t_phase(k, False)
            s_phase(BLOCKS - 1)
            t_phase(BLOCKS - 1, True)

        @block.tensor
        def _(pe):
            def transpose_compact(src, copied=None):
                by_n = src.rearrange("t p c n -> t (p c) n")
                for i in range(TBANKS):
                    if copied is not None:
                        pe.wait_ge(r_done, copied + i + 1)
                    for j in range(GRP):
                        last = nc.tensor.transpose(PA[i][:, j, :], by_n[:, :, GRP * i + j], ident[:, :])
                    last.then_inc(r_full, 1)

            def multiply(bank, weights, moving, full):
                for j in range(GRP):
                    last = nc.tensor.matmul(bank[:, j, :], weights[:, j].rearrange("p q n -> p (q n)"), moving(j),
                                            start=True, stop=True)
                last.then_inc(full, 1)

            def row(buf, t):
                return buf[:, bass.ds(t, 1), :].rearrange("p t s -> p (t s)")

            def column(buf, s):
                return buf[:, :, bass.ds(s, 1)].rearrange("p t s -> p (t s)")

            def t1(i, k, g):
                pe.wait_ge(wa_ready, before_t1(k) + g + 1)
                if not (first(k) and isinstance(g, int) and g < RING):
                    pe.wait_ge(a_done, before_t1(k) + g - RING + 1)
                multiply(PA[i], WA[:, i], lambda j: row(X, GRP * g + j), a_full)

            def s2(i, k, g):
                pe.wait_ge(wa_ready, before_s2(k) + g + 1)
                pe.wait_ge(a_done, before_s2(k) + g - RING + 1)
                pe.wait_ge(b_done, before_s1(k) + g + 1)
                multiply(PA[i], WA[:, i], lambda j: column(Y, GRP * g + j), a_full)

            def s1(i, k, g):
                pe.wait_ge(wb_ready, before_s1(k) + g + 1)
                if not (first(k) and isinstance(g, int) and g < RING):
                    pe.wait_ge(b_done, before_s1(k) + g - RING + 1)
                multiply(PB[i], WB[:, i], lambda j: column(X, GRP * g + j), b_full)

            def t2(i, k, g):
                pe.wait_ge(wb_ready, before_t2(k) + g + 1)
                pe.wait_ge(b_done, before_t2(k) + g - RING + 1)
                multiply(PB[i], WB[:, i], lambda j: row(Y, GRP * g + j), b_full)

            def t1_chunk(k, j):
                if first(k) and j == 0:
                    pe.wait_ge(x_loaded[0], DMA * SPLIT)
                    for g in range(CGROUPS):
                        t1(g % RING, k, g)
                    return
                with pe.Fori(0, CGROUPS // RING) as it:
                    pe.wait_ge(x_loaded[j], DMA * SPLIT * (k + 1))
                    for i in range(RING):
                        t1(i, k, CGROUPS * j + RING * it + i)

            def t2_chunk(k, j):
                with pe.Fori(0, CGROUPS // RING) as it:
                    for i in range(RING):
                        t2(i, k, CGROUPS * j + RING * it + i)

            def s_phase(k):
                for g in range(RING):
                    s1(g, k, g)
                    if g >= LAG:
                        s2(g - LAG, k, g - LAG)
                with pe.Fori(1, GROUPS // RING - 1) as it:
                    for i in range(RING):
                        s1(i, k, RING * it + i)
                        s2((i - LAG) % RING, k, RING * it + i - LAG)
                pe.wait_ge(a_done, before_s2(k) + GROUPS - RING - LAG)
                pe.wait_ge(at_ready, 2 + LAYERS * k)
                transpose_compact(AT[1])
                pe.wait_ge(at_ready, 3 + LAYERS * k)
                transpose_compact(AT[0], before_r(k))
                for g in range(GROUPS - RING, GROUPS):
                    s1(g % RING, k, g)
                    if g == GROUPS - RING:
                        pe.wait_ge(r_done, before_r(k + 1))
                    s2((g - LAG) % RING, k, g - LAG)
                for g in range(GROUPS - LAG, GROUPS):
                    s2(g % RING, k, g)

            pe.wait_ge(consts_ready, 1)
            pe.wait_ge(at_ready, 1)
            transpose_compact(AT[0])
            pe.wait_ge(r_done, TBANKS)
            for j in range(CHUNKS):
                t1_chunk(0, j)
            pe.wait_ge(a_done, GROUPS)
            for l in range(LAYERS):
                pe.wait_ge(as_ready, l + 1)
                transpose_compact(AS[l], TBANKS * l if l else None)
            pe.wait_ge(r_done, before_r(0))

            def block_steps(k):
                s_phase(k)
                t2_chunk(k, 0)
                for j in range(1, CHUNKS):
                    t2_chunk(k, j)
                    t1_chunk(k + 1, j - 1)
                t1_chunk(k + 1, CHUNKS - 1)

            block_steps(0)
            with pe.Fori(1, BLOCKS - 1) as k:
                block_steps(k)
            s_phase(BLOCKS - 1)
            for j in range(CHUNKS):
                t2_chunk(BLOCKS - 1, j)


_LAYER_INPUTS = ['w', 'qw1', 'qw2', 'qdd', 'kw1', 'kw2', 'kdd']


def kernel(**inputs):
    import numpy as _np
    import concourse.bacc as _bacc
    from concourse import mybir as _mybir
    from concourse.bass_utils import run_bass_kernel_spmd as _run

    nc = _bacc.Bacc("TRN2", target_bir_lowering=False, num_devices=1, dynamic_dma_scratch_size=4096)
    arrays, aps = {}, {}
    for name in ['x'] + [f"L{l}_conv_{n}" for l in range(2) for n in _LAYER_INPUTS]:
        a = _np.ascontiguousarray(inputs[name])
        a = a.reshape(a.shape[1:]) if name == 'x' or name.endswith('_w') else a.reshape(a.shape[1], -1)
        arrays[f"in_{name}_dram"] = a
        aps[name] = nc.dram_tensor(f"in_{name}_dram", a.shape, _mybir.dt.from_np(a.dtype),
                                   kind="ExternalInput").ap()
    out = nc.dram_tensor("out_0_dram", (1,) + tuple(arrays["in_x_dram"].shape), _mybir.dt.float32,
                         kind="ExternalOutput").ap()
    cross_conv_kernel(
        nc, aps['x'],
        [tuple(aps[f"L{l}_conv_{n}"] for n in ('qw1', 'qw2', 'qdd')) for l in range(2)],
        [tuple(aps[f"L{l}_conv_{n}"] for n in ('kw1', 'kw2', 'kdd')) for l in range(2)],
        [aps[f"L{l}_conv_w"] for l in range(2)],
        out[0])
    r = _run(nc, [arrays], core_ids=[0])
    return r.results[0]["out_0_dram"]
```

```python
import concourse.bass as bass
from concourse import mybir
from contextlib import ExitStack

P = 128
CH = 16
SPLIT = P // CH
T, S = 1024, 1024
COLS = S // SPLIT
ROWS = 128
BLOCKS = T // ROWS
RANK = 2
LAYERS = 2
GRP = 4
GROUPS = ROWS // GRP
RING = 4
B_SLOTS = 2
AHEAD = B_SLOTS - 1
LAG = 2
CHUNK = RING * GRP
CHUNKS = ROWS // CHUNK
SLOTS = 4
PARAMS = 2 * RANK * CH + CH
DMA = 16
AT_TURNS = (2, 4)
TBANKS = CH // GRP


def cross_conv_kernel(nc, x, row_params, col_params, w, out):
    f32 = mybir.dt.float32
    ALU = mybir.AluOpType
    ACT = mybir.ActivationFunctionType

    ctx = ExitStack()
    with ctx:
        def sb(name, shape):
            return ctx.enter_context(nc.sbuf_tensor(name, shape, f32))

        def sem(name):
            return ctx.enter_context(nc.semaphore(name))

        X = sb("X", [P, ROWS + CHUNK, COLS])
        Y = sb("Y", [P, ROWS + CHUNK, COLS])
        OUT = sb("OUT", [P, SLOTS, CHUNK, COLS])
        RT = [sb(f"RT{l}", [P, ROWS, CH]) for l in range(LAYERS)]
        RS = [sb(f"RS{l}", [P, COLS, CH]) for l in range(LAYERS)]
        WA = sb("WA", [P, RING, GRP, SPLIT, CH])
        WB = sb("WB", [P, B_SLOTS, GRP, SPLIT, CH])
        ident = sb("ident", [P, P])
        mask = sb("mask", [P, SPLIT])
        QP = sb("QP", [P, LAYERS, PARAMS])
        scratch = OUT[:, :, :, :].rearrange("p a b c -> p (a b c)")
        area = SPLIT * CH * CH

        behind = X[:, ROWS:ROWS + CHUNK, :].rearrange("p a b -> p (a b)")

        def part(start, size, of=scratch):
            return of[:, start:start + size]

        AT = [part(l * area, area).rearrange("t (p c n) -> t p c n", p=SPLIT, c=CH) for l in range(LAYERS)]
        AS = [part((1 + l) * area, area).rearrange("s (p c n) -> s p c n", p=SPLIT, c=CH) for l in range(LAYERS)]
        ASTMP = part((1 + LAYERS) * area, area).rearrange("s (p c n) -> s p c n", p=SPLIT, c=CH)
        PROD = part(LAYERS * area, RANK * CH * CH).rearrange("t (i c n) -> t i c n", i=RANK, c=CH)
        KP = [part(l * SPLIT * PARAMS, SPLIT * PARAMS, behind).rearrange("s (p v) -> s p v", p=SPLIT)
              for l in range(LAYERS)]
        WI = [part(LAYERS * SPLIT * PARAMS + l * CH * CH, CH * CH, behind)
              .rearrange("s (c n) -> s c n", c=CH) for l in range(LAYERS)]

        PA = [ctx.enter_context(nc.psum_tensor(f"PA{i}", [P, GRP, P], f32)) for i in range(RING)]
        PB = [ctx.enter_context(nc.psum_tensor(f"PB{i}", [P, GRP, P], f32)) for i in range(RING)]

        x_loaded = [sem(f"x_loaded{j}") for j in range(CHUNKS)]
        q_loaded = sem("q_loaded")
        k_loaded = sem("k_loaded")
        consts_ready = sem("consts_ready")
        pool_step = sem("pool_step")
        dve_step = sem("dve_step")
        at_step = sem("at_step")
        at_ready = sem("at_ready")
        as_ready = sem("as_ready")
        r_full = sem("r_full")
        r_done = sem("r_done")
        wa_ready = sem("wa_ready")
        wb_ready = sem("wb_ready")
        a_full = sem("a_full")
        a_done = sem("a_done")
        b_full = sem("b_full")
        b_done = sem("b_done")
        stored = [sem(f"stored{b}") for b in range(2)]

        def before_t1(k):
            return 2 * GROUPS * k

        def before_s2(k):
            return 2 * GROUPS * k + GROUPS

        def before_s1(k):
            return 2 * GROUPS * k

        def before_t2(k):
            return 2 * GROUPS * k + GROUPS

        def before_r(k):
            return TBANKS + LAYERS * TBANKS + LAYERS * TBANKS * k

        def place(k):
            return CHUNK * (k % 2), ROWS * (k % 2)

        def chunk_at(k, j):
            return CHUNK * j if j else place(k)[1]

        def t2_chunk_at(o):
            return (o + 1) % CHUNKS

        def stores_of(k, o, half):
            starts = ((0, 4), (2, 6, 7))[half]
            return DMA * SPLIT * (len(starts) * k + sum(start < o - o % 2 for start in starts))

        def first(k):
            return isinstance(k, int) and k == 0

        def columns(buf, k, s):
            return buf[:, bass.ds(place(k)[0], ROWS), bass.ds(s, GRP)].rearrange("p t s -> p s t")

        def rows(buf, t):
            return buf[:, bass.ds(t, GRP), :]

        def spread(engine, dst, compact, at, ready):
            r = compact[:, bass.ds(at, GRP), :].unsqueeze(2).broadcast_to([P, GRP, SPLIT, CH])
            m = mask[:, :].unsqueeze(1).unsqueeze(3).broadcast_to([P, GRP, SPLIT, CH])
            engine.tensor_tensor(dst, r, m, ALU.mult).then_inc(ready, 1)

        block = ctx.enter_context(nc.Block())

        @block.sync
        def _(sp):
            def load_rows(l, k):
                w1, w2, dd = row_params[l]
                for src, at, size in ((w1, 0, RANK * CH), (w2, RANK * CH, RANK * CH), (dd, 2 * RANK * CH, CH)):
                    sp.dma_start(QP[:, l, at:at + size], src[bass.ds(k * ROWS, ROWS), :]).then_inc(q_loaded, DMA)

            def load_x(k, j):
                for p in range(SPLIT):
                    sp.dma_start(X[CH * p:CH * (p + 1), bass.ds(chunk_at(k, j), CHUNK), :],
                                 x[:, bass.ds(k * ROWS + CHUNK * j, CHUNK), COLS * p:COLS * (p + 1)]
                                 ).then_inc(x_loaded[j], DMA)

            def store(k, o, chunks):
                slot = o % SLOTS
                for p in range(SPLIT):
                    sp.dma_start(out[:, bass.ds(k * ROWS + CHUNK * t2_chunk_at(o), CHUNK * chunks),
                                     COLS * p:COLS * (p + 1)],
                                 OUT[CH * p:CH * (p + 1), slot:slot + chunks, :, :].rearrange(
                                     "c h t s -> c (h t) s")).then_inc(stored[slot // 2], DMA)

            def block_steps(k, loads, load_ahead):
                for o in range(CHUNKS):
                    sp.wait_ge(b_done, before_t2(k) + RING * (o + 1))
                    if loads and o + 1 < CHUNKS:
                        load_x(k + 1, o + 1)
                    if o >= CHUNKS - 2:
                        store(k, o, 1)
                    elif o % 2:
                        store(k, o - 1, 2)
                if loads:
                    sp.wait_ge(at_ready, 1 + LAYERS * (k + 1))
                    load_rows(1, k + 1)
                    load_rows(0, (k + 2) % BLOCKS)
                if load_ahead:
                    load_x(k + 2, 0)

            load_rows(0, 0)
            for j in range(CHUNKS):
                load_x(0, j)
            sp.wait_ge(at_ready, 1)
            load_rows(1, 0)
            load_rows(0, 1)
            sp.wait_ge(as_ready, LAYERS)
            sp.wait_ge(a_full, RING)
            load_x(1, 0)
            with sp.Fori(0, BLOCKS - 2) as k:
                block_steps(k, True, True)
            block_steps(BLOCKS - 2, True, False)
            block_steps(BLOCKS - 1, False, False)
            for half in range(2):
                sp.wait_ge(stored[half], stores_of(BLOCKS, 0, half))

        @block.gpsimd
        def _(pool):
            nc.gpsimd.memset(ident[:, :], 0.0).then_inc(pool_step, 1)
            nc.gpsimd.memset(mask[:, :], 1.0).then_inc(pool_step, 1)
            pool.wait_ge(pool_step, 2)
            nc.gpsimd.affine_select(out=ident[:, :], in_=ident[:, :], compare_op=ALU.not_equal, fill=1.0,
                                    base=0, pattern=[[-1, P]], channel_multiplier=1).then_inc(consts_ready, 1)
            nc.gpsimd.affine_select(out=mask[:, :], in_=mask[:, :], compare_op=ALU.is_ge, fill=0.0,
                                    base=0, pattern=[[-CH, SPLIT]], channel_multiplier=1).then_inc(pool_step, 1)
            pool.wait_ge(pool_step, 3)
            nc.gpsimd.affine_select(out=mask[:, :], in_=mask[:, :], compare_op=ALU.is_ge, fill=0.0,
                                    base=CH - 1, pattern=[[CH, SPLIT]], channel_multiplier=-1
                                    ).then_inc(consts_ready, 1)
            pool.wait_ge(consts_ready, 2)

            def row_matrices(l, before):
                shape = [P, CH, CH]
                q1, q2 = ([QP[:, l, (RANK * j + i) * CH:(RANK * j + i + 1) * CH] for i in range(RANK)]
                          for j in range(2))
                for i in range(RANK):
                    nc.gpsimd.tensor_tensor(PROD[:, i], q1[i].unsqueeze(2).broadcast_to(shape),
                                            q2[i].unsqueeze(1).broadcast_to(shape), ALU.mult).then_inc(at_step, 1)
                pool.wait_ge(at_step, before + RANK)
                diagonal = PROD[:, 0].rearrange("t c n -> t (c n)")[:, 0:CH * CH:CH + 1]
                nc.gpsimd.tensor_tensor(diagonal, diagonal, QP[:, l, 2 * RANK * CH:PARAMS], ALU.add
                                        ).then_inc(at_step, 1)
                pool.wait_ge(at_step, before + RANK + 1)
                wide = [P, SPLIT, CH * CH]
                flat = [PROD[:, i].rearrange("t c n -> t (c n)").unsqueeze(1).broadcast_to(wide) for i in range(RANK)]
                nc.gpsimd.tensor_tensor(AT[l].rearrange("t p c n -> t p (c n)"), flat[0], flat[1], ALU.add
                                        ).then_inc(at_ready, 1)

            def row_matrices_of(k, l):
                steps = RANK + 1
                n = (1, 0).index(l)
                pool.wait_ge(q_loaded, DMA * 3 * (1 + LAYERS) + DMA * 3 * LAYERS * k)
                if first(k):
                    pool.wait_ge(r_full, before_r(0))
                else:
                    for half in range(2):
                        pool.wait_ge(stored[half], stores_of(k, 0, half))
                pool.wait_ge(at_ready, 1 + n + LAYERS * k)
                row_matrices(l, steps * (1 + n) + steps * LAYERS * k)

            pool.wait_ge(q_loaded, DMA * 3)
            row_matrices(0, 0)

            pool.wait_ge(r_done, TBANKS)
            for i in range(RING):
                spread(nc.gpsimd, WA[:, i], RT[0], GRP * i, wa_ready)
            with pool.Fori(1, GROUPS // RING) as it:
                for i in range(RING):
                    pool.wait_ge(a_full, RING * it + i - RING + 1)
                    spread(nc.gpsimd, WA[:, i], RT[0], GRP * (RING * it + i), wa_ready)

            def phase(compact, before, start, end, copied):
                with pool.Fori(start, end) as it:
                    pool.wait_ge(r_done, copied)
                    for i in range(RING):
                        pool.wait_ge(a_full, before + RING * it + i - RING + 1)
                        spread(nc.gpsimd, WA[:, i], compact, GRP * (RING * it + i), wa_ready)

            def s2_weights(k):
                phase(RS[1], before_s2(k), 0, AT_TURNS[0], before_r(k))
                row_matrices_of(k, 1)
                phase(RS[1], before_s2(k), *AT_TURNS, before_r(k))
                row_matrices_of(k, 0)
                phase(RS[1], before_s2(k), AT_TURNS[1], GROUPS // RING, before_r(k))

            def t1_weights(k):
                phase(RT[0], before_t1(k), 0, GROUPS // RING, before_r(k))

            s2_weights(0)
            t1_weights(1)
            with pool.Fori(1, BLOCKS - 1) as k:
                s2_weights(k)
                t1_weights(k + 1)
            s2_weights(BLOCKS - 1)

        @block.scalar
        def _(act):
            for l in range(LAYERS):
                w1, w2, dd = col_params[l]
                for src, at, size in ((w1, 0, RANK * CH), (w2, RANK * CH, RANK * CH), (dd, 2 * RANK * CH, CH)):
                    act.dma_start(KP[l][:, :, at:at + size], src.rearrange("(p s) v -> s p v", p=SPLIT)
                                  ).then_inc(k_loaded, DMA)
                act.dma_start(WI[l], w[l].unsqueeze(0).broadcast_to([P, CH, CH])).then_inc(k_loaded, DMA)

            def copy_compact(dst, before):
                for i in range(TBANKS):
                    act.wait_ge(r_full, before + i + 1)
                    nc.scalar.activation(dst[:, :, :].rearrange("p t n -> p n t")[:, GRP * i:GRP * (i + 1), :],
                                         PA[i][:, :, :], ACT.Copy).then_inc(r_done, 1)

            def t1_copies(k):
                for i in range(RING):
                    act.wait_ge(a_full, before_t1(k) + i + 1)
                    nc.scalar.activation(rows(Y, chunk_at(k, 0) + GRP * i), PA[i][:, :, :], ACT.Copy
                                         ).then_inc(a_done, 1)
                with act.Fori(1, CHUNKS) as j:
                    for i in range(RING):
                        act.wait_ge(a_full, before_t1(k) + RING * j + i + 1)
                        nc.scalar.activation(rows(Y, CHUNK * j + GRP * i), PA[i][:, :, :], ACT.Copy
                                             ).then_inc(a_done, 1)

            copy_compact(RT[0], 0)
            t1_copies(0)
            for l in range(LAYERS):
                copy_compact(RS[l], TBANKS * (1 + l))

            def s_phase(k):
                def copy(i, g):
                    act.wait_ge(a_full, before_s2(k) + g + 1)
                    nc.scalar.activation(columns(X, k, GRP * g), PA[i][:, :, :], ACT.Copy).then_inc(a_done, 1)

                turns = (GROUPS - RING - LAG) // RING
                with act.Fori(0, turns) as it:
                    for i in range(RING):
                        copy(i, RING * it + i)
                for g in range(RING * turns, GROUPS - RING - LAG):
                    copy(g % RING, g)
                act.wait_ge(wa_ready, before_s2(k))
                if not first(k):
                    act.wait_ge(wb_ready, before_s1(k))
                copy_compact(RT[1], before_r(k))
                copy_compact(RT[0], before_r(k) + TBANKS)
                for g in range(GROUPS - RING - LAG, GROUPS):
                    copy(g % RING, g)

            def block_steps(k):
                s_phase(k)
                t1_copies(k + 1)

            block_steps(0)
            with act.Fori(1, BLOCKS - 1) as k:
                block_steps(k)
            s_phase(BLOCKS - 1)

        @block.vector
        def _(dve):
            step = [0]

            def chained(instruction):
                step[0] += 1
                instruction.then_inc(dve_step, 1)
                dve.wait_ge(dve_step, step[0])

            def column_matrices(l):
                shape = [P, SPLIT, CH, CH]
                kw = [[KP[l][:, :, (RANK * j + i) * CH:(RANK * j + i + 1) * CH] for i in range(RANK)]
                      for j in range(2)]
                dd = KP[l][:, :, 2 * RANK * CH:PARAMS]
                for i in range(RANK):
                    chained(nc.vector.tensor_tensor((AS[l], ASTMP)[i], kw[0][i].unsqueeze(3).broadcast_to(shape),
                                                    kw[1][i].unsqueeze(2).broadcast_to(shape), ALU.mult))
                chained(nc.vector.tensor_tensor(AS[l], AS[l], ASTMP, ALU.add))
                diagonal = AS[l].rearrange("s p c n -> s p (c n)")[:, :, 0:CH * CH:CH + 1]
                chained(nc.vector.tensor_tensor(diagonal, diagonal, dd, ALU.add))
                wi = WI[l].rearrange("s c n -> s (c n)")
                chained(nc.vector.tensor_scalar(wi[:, 0:CH * CH:CH + 1], wi[:, 0:CH * CH:CH + 1], 1.0, None,
                                                ALU.add))
                nc.vector.tensor_tensor(AS[l], AS[l], WI[l].unsqueeze(1).broadcast_to(shape), ALU.add
                                        ).then_inc(as_ready, 1)

            def add_columns(i, k, g):
                dve.wait_ge(b_full, before_s1(k) + g + 1)
                at = columns(Y, k, GRP * g)
                nc.vector.tensor_tensor(at, PB[i][:, :, :], at, ALU.add).then_inc(b_done, 1)

            def add_rows(i, k, o):
                dve.wait_ge(b_full, before_t2(k) + RING * o + i + 1)
                nc.vector.tensor_tensor(OUT[:, o % SLOTS, GRP * i:GRP * (i + 1), :], PB[i][:, :, :],
                                        rows(X, chunk_at(k, t2_chunk_at(o)) + GRP * i), ALU.add).then_inc(b_done, 1)

            def t2_weights(slot, g):
                row = CHUNK * t2_chunk_at(g // RING) + GRP * (g % RING)
                spread(nc.vector, WB[:, slot], RT[1], row, wb_ready)

            def s_phase(k):
                with dve.Fori(0, GROUPS // RING - 1) as it:
                    dve.wait_ge(a_done, before_s2(k))
                    for i in range(RING):
                        spread(nc.vector, WB[:, (i + AHEAD) % B_SLOTS], RS[0], GRP * (RING * it + i + AHEAD), wb_ready)
                        add_columns(i, k, RING * it + i)
                for i in range(RING):
                    g = GROUPS - RING + i + AHEAD
                    if g == GROUPS:
                        dve.wait_ge(r_done, before_r(k) + TBANKS)
                    if g < GROUPS:
                        spread(nc.vector, WB[:, (i + AHEAD) % B_SLOTS], RS[0], GRP * g, wb_ready)
                    else:
                        t2_weights((i + AHEAD) % B_SLOTS, g - GROUPS)
                    add_columns(i, k, GROUPS - RING + i)

            def t_phase(k, last):
                dve.wait_ge(a_done, before_t1(k + 1))
                dve.wait_ge(r_full, before_r(k + 1))
                for o in range(CHUNKS):
                    if o >= SLOTS or not first(k):
                        half = o % SLOTS // 2
                        dve.wait_ge(stored[half], stores_of(k, o, half))
                    for i in range(RING):
                        g = RING * o + i + AHEAD
                        if g < GROUPS:
                            t2_weights((i + AHEAD) % B_SLOTS, g)
                        elif not last:
                            spread(nc.vector, WB[:, (i + AHEAD) % B_SLOTS], RS[0], GRP * (g - GROUPS), wb_ready)
                        add_rows(i, k, o)

            dve.wait_ge(k_loaded, DMA * 4 * LAYERS)
            for l in range(LAYERS):
                dve.wait_ge(at_ready, 1)
                column_matrices(l)
                dve.wait_ge(as_ready, l + 1)
            dve.wait_ge(consts_ready, 2)
            dve.wait_ge(r_done, 2 * TBANKS)
            for i in range(AHEAD):
                spread(nc.vector, WB[:, i], RS[0], GRP * i, wb_ready)
            s_phase(0)
            t_phase(0, False)
            with dve.Fori(1, BLOCKS - 1) as k:
                s_phase(k)
                t_phase(k, False)
            s_phase(BLOCKS - 1)
            t_phase(BLOCKS - 1, True)

        @block.tensor
        def _(pe):
            def transpose_compact(src, copied=None):
                by_n = src.rearrange("t p c n -> t (p c) n")
                for i in range(TBANKS):
                    if copied is not None:
                        pe.wait_ge(r_done, copied + i + 1)
                    for j in range(GRP):
                        last = nc.tensor.transpose(PA[i][:, j, :], by_n[:, :, GRP * i + j], ident[:, :])
                    last.then_inc(r_full, 1)

            def multiply(bank, weights, moving, full):
                for j in range(GRP):
                    last = nc.tensor.matmul(bank[:, j, :], weights[:, j].rearrange("p q n -> p (q n)"), moving(j),
                                            start=True, stop=True)
                last.then_inc(full, 1)

            def row(buf, t):
                return buf[:, bass.ds(t, 1), :].rearrange("p t s -> p (t s)")

            def column(buf, k, s):
                return buf[:, bass.ds(place(k)[0], ROWS), bass.ds(s, 1)].rearrange("p t s -> p (t s)")

            def t1(i, k, j):
                if i == 0:
                    pe.wait_ge(x_loaded[j], DMA * SPLIT * (k + 1))
                g = RING * j + i
                pe.wait_ge(wa_ready, before_t1(k) + g + 1)
                if g >= RING or not first(k):
                    pe.wait_ge(a_done, before_t1(k) + g - RING + 1)
                multiply(PA[i], WA[:, i], lambda r: row(X, chunk_at(k, j) + GRP * i + r), a_full)

            def s2(i, k, g):
                pe.wait_ge(wa_ready, before_s2(k) + g + 1)
                pe.wait_ge(a_done, before_s2(k) + g - RING + 1)
                pe.wait_ge(b_done, before_s1(k) + g + 1)
                multiply(PA[i], WA[:, i], lambda r: column(Y, k, GRP * g + r), a_full)

            def s1(i, k, g):
                pe.wait_ge(wb_ready, before_s1(k) + g + 1)
                if not (first(k) and isinstance(g, int) and g < RING):
                    pe.wait_ge(b_done, before_s1(k) + g - RING + 1)
                multiply(PB[i], WB[:, i % B_SLOTS], lambda r: column(X, k, GRP * g + r), b_full)

            def t2(i, k, o):
                g = RING * o + i
                pe.wait_ge(wb_ready, before_t2(k) + g + 1)
                pe.wait_ge(b_done, before_t2(k) + g - RING + 1)
                multiply(PB[i], WB[:, i % B_SLOTS], lambda r: row(Y, chunk_at(k, t2_chunk_at(o)) + GRP * i + r), b_full)

            def s_phase(k):
                for g in range(RING):
                    s1(g, k, g)
                    if g >= LAG:
                        s2(g - LAG, k, g - LAG)
                with pe.Fori(1, GROUPS // RING - 1) as it:
                    for i in range(RING):
                        s1(i, k, RING * it + i)
                        s2((i - LAG) % RING, k, RING * it + i - LAG)
                pe.wait_ge(a_done, before_s2(k) + GROUPS - RING - LAG)
                pe.wait_ge(at_ready, 2 + LAYERS * k)
                transpose_compact(AT[1])
                pe.wait_ge(at_ready, 3 + LAYERS * k)
                transpose_compact(AT[0], before_r(k))
                for g in range(GROUPS - RING, GROUPS):
                    s1(g % RING, k, g)
                    if g == GROUPS - RING:
                        pe.wait_ge(r_done, before_r(k + 1))
                    s2((g - LAG) % RING, k, g - LAG)
                for g in range(GROUPS - LAG, GROUPS):
                    s2(g % RING, k, g)

            pe.wait_ge(consts_ready, 1)
            pe.wait_ge(at_ready, 1)
            transpose_compact(AT[0])
            pe.wait_ge(r_done, TBANKS)
            for j in range(CHUNKS):
                for i in range(RING):
                    t1(i, 0, j)
            pe.wait_ge(a_done, GROUPS)
            for l in range(LAYERS):
                pe.wait_ge(as_ready, l + 1)
                transpose_compact(AS[l], TBANKS * l if l else None)
            pe.wait_ge(r_done, before_r(0))

            def block_steps(k):
                s_phase(k)
                for o in range(CHUNKS + 1):
                    for i in range(RING):
                        if o < CHUNKS:
                            t2(i, k, o)
                        if o > 0:
                            t1(i, k + 1, o - 1)

            block_steps(0)
            with pe.Fori(1, BLOCKS - 1) as k:
                block_steps(k)
            s_phase(BLOCKS - 1)
            for o in range(CHUNKS):
                for i in range(RING):
                    t2(i, BLOCKS - 1, o)


_LAYER_INPUTS = ['w', 'qw1', 'qw2', 'qdd', 'kw1', 'kw2', 'kdd']


def kernel(**inputs):
    import numpy as _np
    import concourse.bacc as _bacc
    from concourse import mybir as _mybir
    from concourse.bass_utils import run_bass_kernel_spmd as _run

    nc = _bacc.Bacc("TRN2", target_bir_lowering=False, num_devices=1, dynamic_dma_scratch_size=1024)
    arrays, aps = {}, {}
    for name in ['x'] + [f"L{l}_conv_{n}" for l in range(2) for n in _LAYER_INPUTS]:
        a = _np.ascontiguousarray(inputs[name])
        a = a.reshape(a.shape[1:]) if name == 'x' or name.endswith('_w') else a.reshape(a.shape[1], -1)
        arrays[f"in_{name}_dram"] = a
        aps[name] = nc.dram_tensor(f"in_{name}_dram", a.shape, _mybir.dt.from_np(a.dtype),
                                   kind="ExternalInput").ap()
    out = nc.dram_tensor("out_0_dram", (1,) + tuple(arrays["in_x_dram"].shape), _mybir.dt.float32,
                         kind="ExternalOutput").ap()
    cross_conv_kernel(
        nc, aps['x'],
        [tuple(aps[f"L{l}_conv_{n}"] for n in ('qw1', 'qw2', 'qdd')) for l in range(2)],
        [tuple(aps[f"L{l}_conv_{n}"] for n in ('kw1', 'kw2', 'kdd')) for l in range(2)],
        [aps[f"L{l}_conv_w"] for l in range(2)],
        out[0])
    r = _run(nc, [arrays], core_ids=[0])
    return r.results[0]["out_0_dram"]
```

```python
import concourse.bass as bass
from concourse import mybir
from contextlib import ExitStack

P = 128
CH = 16
SPLIT = P // CH
T, S = 1024, 1024
COLS = S // SPLIT
ROWS = 128
BLOCKS = T // ROWS
RANK = 2
LAYERS = 2
GRP = 4
GROUPS = ROWS // GRP
RING = 4
B_SLOTS = 2
LAG = 2
CHUNK = RING * GRP
CHUNKS = ROWS // CHUNK
SLOTS = 4
PARAMS = 2 * RANK * CH + CH
EARLY = B_SLOTS
DMA = 16

PROD_TURNS = (2, 3)
R_TURN = 4
R_GROUP = RING * R_TURN - LAG + 1
R_BANK = R_GROUP % RING
HALVES = CH * CH // P
RT_ROWS = ROWS // RING
TBANKS = CH // GRP

COLUMN_LOADS = (0, 2)
RS_CHUNKS = (4, 7)
DVE_T2 = [g for g in range(GROUPS) if g < EARLY or g % 3 == 1]
POOL_T2 = [g for g in range(GROUPS) if g not in DVE_T2]


def cross_conv_kernel(nc, x, row_params, col_params, w, out):
    f32 = mybir.dt.float32
    ALU = mybir.AluOpType
    ACT = mybir.ActivationFunctionType

    ctx = ExitStack()
    with ctx:
        def sb(name, shape):
            return ctx.enter_context(nc.sbuf_tensor(name, shape, f32))

        def sem(name):
            return ctx.enter_context(nc.semaphore(name))

        X = sb("X", [P, ROWS + CHUNK, COLS])
        Y = sb("Y", [P, ROWS + CHUNK, COLS])
        OUT = sb("OUT", [P, SLOTS, CHUNK, COLS])
        RT = sb("RT", [P, LAYERS, ROWS, CH])
        RS = sb("RS", [P, LAYERS, COLS, CH])
        WA = sb("WA", [P, RING, GRP, SPLIT, CH])
        WB = sb("WB", [P, B_SLOTS, GRP, SPLIT, CH])
        ident = sb("ident", [P, P])
        mask = sb("mask", [P, SPLIT])
        QP = sb("QP", [P, LAYERS, PARAMS])
        warm = sb("warm", [P, 1])
        scratch = OUT[:, :, :, :].rearrange("p a b c -> p (a b c)")
        area = SPLIT * CH * CH

        behind = X[:, ROWS:ROWS + CHUNK, :].rearrange("p a b -> p (a b)")

        def part(start, size, of=scratch):
            return of[:, start:start + size]

        AT = part(0, area).rearrange("t (p c n) -> t p c n", p=SPLIT, c=CH)
        AS = [part((1 + l) * area, area).rearrange("s (p c n) -> s p c n", p=SPLIT, c=CH) for l in range(LAYERS)]
        ASTMP = part((1 + LAYERS) * area, area).rearrange("s (p c n) -> s p c n", p=SPLIT, c=CH)
        PROD = [part(LAYERS * area + l * RANK * CH * CH, RANK * CH * CH)
                .rearrange("t (i c n) -> t i c n", i=RANK, c=CH) for l in range(LAYERS)]
        RC = part(LAYERS * area + LAYERS * RANK * CH * CH, LAYERS * HALVES * ROWS).rearrange(
            "q (l h t) -> q l h t", l=LAYERS, h=HALVES)
        RN = part(0, LAYERS * CH * ROWS)
        KP = [part(l * SPLIT * PARAMS, SPLIT * PARAMS, behind).rearrange("s (p v) -> s p v", p=SPLIT)
              for l in range(LAYERS)]
        WI = [part(LAYERS * SPLIT * PARAMS + l * CH * CH, CH * CH, behind)
              .rearrange("s (c n) -> s c n", c=CH) for l in range(LAYERS)]

        PA = [ctx.enter_context(nc.psum_tensor(f"PA{i}", [P, GRP, P], f32)) for i in range(RING)]
        PB = [ctx.enter_context(nc.psum_tensor(f"PB{i}", [P, GRP, P], f32)) for i in range(RING)]

        x_loaded = [sem(f"x_loaded{j}") for j in range(CHUNKS)]
        q_loaded = sem("q_loaded")
        k_loaded = [sem(f"k_loaded{l}") for l in range(LAYERS)]
        consts_ready = sem("consts_ready")
        pool_step = sem("pool_step")
        dve_step = sem("dve_step")
        act_step = sem("act_step")
        prod_step = sem("prod_step")
        prod_ready = sem("prod_ready")
        at_ready = sem("at_ready")
        as_ready = sem("as_ready")
        r_full = sem("r_full")
        r_done = sem("r_done")
        rn_loaded = sem("rn_loaded")
        rt_ready = sem("rt_ready")
        wa_ready = sem("wa_ready")
        wb_ready = sem("wb_ready")
        a_full = sem("a_full")
        a_done = sem("a_done")
        b_full = sem("b_full")
        b_done = sem("b_done")
        stored = [sem(f"stored{n}") for n in range(3)]

        def before_t1(k):
            return 2 * GROUPS * k

        def before_s2(k):
            return 2 * GROUPS * k + GROUPS

        def before_s1(k):
            return 2 * GROUPS * k

        def before_t2(k):
            return 2 * GROUPS * k + GROUPS

        def before_r(k):
            return TBANKS + LAYERS * TBANKS + k

        REPEATS = SPLIT.bit_length() - 1
        RN_DMAS = LAYERS * HALVES + REPEATS

        def rt_there(k, layers=LAYERS):
            return RING * (LAYERS * k + layers)

        def wa_count(groups):
            return groups - CHUNKS

        def wb_count(groups):
            return groups + CHUNKS

        def place(k):
            return CHUNK * (k % 2), ROWS * (k % 2)

        def chunk_at(k, j):
            return CHUNK * j if j else place(k)[1]

        def t2_chunk_at(o):
            return (o + 1) % CHUNKS

        def stores_of(k, o, slots):
            for n, (starts, of) in enumerate((((0, 4), (0, 1)), ((2, 6), (2, 3)), ((7,), (3,)))):
                done = DMA * SPLIT * (len(starts) * k + sum(start < o - o % 2 for start in starts))
                if set(of) & set(slots) and not (isinstance(done, int) and done == 0):
                    yield stored[n], done

        def t2_before_t1(g):
            return min(GROUPS, 2 * (g + 1) if g < RING else g + RING + 3)

        def first(k):
            return isinstance(k, int) and k == 0

        def columns(buf, k, s):
            return buf[:, bass.ds(place(k)[0], ROWS), bass.ds(s, GRP)].rearrange("p t s -> p s t")

        def rows(buf, t):
            return buf[:, bass.ds(t, GRP), :]

        def spread(engine, dst, compact, at, ready):
            r = compact[:, bass.ds(at, GRP), :].unsqueeze(2).broadcast_to([P, GRP, SPLIT, CH])
            m = mask[:, :].unsqueeze(1).unsqueeze(3).broadcast_to([P, GRP, SPLIT, CH])
            engine.tensor_tensor(dst, r, m, ALU.mult).then_inc(ready, 1)

        block = ctx.enter_context(nc.Block())

        @block.sync
        def _(sp):
            def load_rows(l, k):
                w1, w2, dd = row_params[l]
                for src, at, size in ((w1, 0, RANK * CH), (w2, RANK * CH, RANK * CH), (dd, 2 * RANK * CH, CH)):
                    sp.dma_start(QP[:, l, at:at + size], src[bass.ds(k * ROWS, ROWS), :]).then_inc(q_loaded, DMA)

            def load_x(k, j):
                for p in range(SPLIT):
                    sp.dma_start(X[CH * p:CH * (p + 1), bass.ds(chunk_at(k, j), CHUNK), :],
                                 x[:, bass.ds(k * ROWS + CHUNK * j, CHUNK), COLS * p:COLS * (p + 1)]
                                 ).then_inc(x_loaded[j], DMA)

            def store(k, o, chunks):
                slot = o % SLOTS
                for p in range(SPLIT):
                    sp.dma_start(out[:, bass.ds(k * ROWS + CHUNK * t2_chunk_at(o), CHUNK * chunks),
                                     COLS * p:COLS * (p + 1)],
                                 OUT[CH * p:CH * (p + 1), slot:slot + chunks, :, :].rearrange(
                                     "c h t s -> c (h t) s")).then_inc(stored[2 if o == 7 else slot // 2], DMA)

            def load_compact(k):
                done = 0
                sp.wait_ge(r_done, before_r(k) + 1)
                for l in range(LAYERS):
                    for h in range(HALVES):
                        c = CH // HALVES
                        sp.dma_start(RN[c * h:c * (h + 1), CH * ROWS * l:CH * ROWS * (l + 1)].rearrange(
                            "c (n t) -> c n t", n=CH), RC[:, l, h, :]).then_inc(rn_loaded, DMA)
                        done += 1
                for r in range(REPEATS):
                    sp.wait_ge(rn_loaded, DMA * (RN_DMAS * k + done))
                    size = CH << r
                    sp.dma_start(RN[size:2 * size, :], RN[0:size, :]).then_inc(rn_loaded, DMA)
                    done += 1

            def block_steps(k, loads, load_ahead):
                load_compact(k)
                for o in range(CHUNKS):
                    sp.wait_ge(b_done, before_t2(k) + RING * (o + 1))
                    if loads and o + 1 < CHUNKS:
                        load_x(k + 1, o + 1)
                    if o in (1, 3) or o == 5 and not loads:
                        store(k, o - 1, 2)
                    elif o == 6 and loads:
                        store(k, 4, 2)
                    if o >= 6:
                        store(k, o, 1)
                if loads:
                    sp.wait_ge(prod_ready, LAYERS * (k + 1))
                    load_rows(1, k + 1)
                    load_rows(0, (k + 2) % BLOCKS)
                if load_ahead:
                    load_x(k + 2, 0)

            def load_columns(l):
                w1, w2, dd = col_params[l]
                for src, at, size in ((w1, 0, RANK * CH), (w2, RANK * CH, RANK * CH), (dd, 2 * RANK * CH, CH)):
                    sp.dma_start(KP[l][:, :, at:at + size], src.rearrange("(p s) v -> s p v", p=SPLIT)
                                 ).then_inc(k_loaded[l], DMA)
                sp.dma_start(WI[l], w[l].unsqueeze(0).broadcast_to([P, CH, CH])).then_inc(k_loaded[l], DMA)

            load_rows(0, 0)
            for j in range(CHUNKS):
                load_x(0, j)
                if j in COLUMN_LOADS:
                    load_columns(COLUMN_LOADS.index(j))
            sp.wait_ge(at_ready, TBANKS)
            load_rows(1, 0)
            load_rows(0, 1)
            sp.wait_ge(as_ready, LAYERS)
            sp.wait_ge(a_full, RING)
            load_x(1, 0)
            block_steps(0, True, True)
            with sp.Fori(1, BLOCKS - 2) as k:
                block_steps(k, True, True)
            block_steps(BLOCKS - 2, True, False)
            block_steps(BLOCKS - 1, False, False)
            for semaphore, done in stores_of(BLOCKS, 0, range(SLOTS)):
                sp.wait_ge(semaphore, done)

        @block.gpsimd
        def _(pool):
            nc.gpsimd.memset(ident[:, :], 0.0).then_inc(pool_step, 1)
            nc.gpsimd.memset(mask[:, :], 1.0).then_inc(pool_step, 1)
            pool.wait_ge(pool_step, 2)
            nc.gpsimd.affine_select(out=ident[:, :], in_=ident[:, :], compare_op=ALU.not_equal, fill=1.0,
                                    base=0, pattern=[[-1, P]], channel_multiplier=1).then_inc(consts_ready, 1)
            nc.gpsimd.affine_select(out=mask[:, :], in_=mask[:, :], compare_op=ALU.is_ge, fill=0.0,
                                    base=0, pattern=[[-CH, SPLIT]], channel_multiplier=1).then_inc(pool_step, 1)
            pool.wait_ge(pool_step, 3)
            nc.gpsimd.affine_select(out=mask[:, :], in_=mask[:, :], compare_op=ALU.is_ge, fill=0.0,
                                    base=CH - 1, pattern=[[CH, SPLIT]], channel_multiplier=-1
                                    ).then_inc(consts_ready, 1)
            pool.wait_ge(consts_ready, 2)

            def row_matrices(l, before):
                shape = [P, CH, CH]
                q1, q2 = ([QP[:, l, (RANK * j + i) * CH:(RANK * j + i + 1) * CH] for i in range(RANK)]
                          for j in range(2))
                prod = PROD[l]
                for i in range(RANK):
                    nc.gpsimd.tensor_tensor(prod[:, i], q1[i].unsqueeze(2).broadcast_to(shape),
                                            q2[i].unsqueeze(1).broadcast_to(shape), ALU.mult
                                            ).then_inc(prod_step, 1)
                pool.wait_ge(prod_step, before + RANK)
                nc.gpsimd.tensor_tensor(prod[:, 0], prod[:, 0], prod[:, 1], ALU.add).then_inc(prod_step, 1)
                pool.wait_ge(prod_step, before + RANK + 1)
                diagonal = prod[:, 0].rearrange("t c n -> t (c n)")[:, 0:CH * CH:CH + 1]
                nc.gpsimd.tensor_tensor(diagonal, diagonal, QP[:, l, 2 * RANK * CH:PARAMS], ALU.add
                                        ).then_inc(prod_ready, 1)

            def layer1_matrices(k):
                pool.wait_ge(q_loaded, DMA * 3 * (1 + LAYERS) + DMA * 3 * LAYERS * k)
                pool.wait_ge(r_full, before_r(k))
                for semaphore, done in stores_of(k, 0, [0, 1, 2]):
                    pool.wait_ge(semaphore, done)
                row_matrices(1, (RANK + 1) * LAYERS * k)

            def layer0_matrices(k):
                row_matrices(0, (RANK + 1) * (LAYERS * k + 1))

            pool.wait_ge(r_done, TBANKS)
            for i in range(1, RING):
                spread(nc.gpsimd, WA[:, i], RT[:, 0], GRP * i, wa_ready)
            with pool.Fori(1, GROUPS // RING) as it:
                for i in range(1, RING):
                    pool.wait_ge(a_full, RING * it + i - RING + 1)
                    spread(nc.gpsimd, WA[:, i], RT[:, 0], GRP * (RING * it + i), wa_ready)

            def phase(compact, before, start, end, there, count):
                with pool.Fori(start, end) as it:
                    pool.wait_ge(there, count)
                    for i in range(RING):
                        pool.wait_ge(a_full, before + RING * it + i - RING + 1)
                        spread(nc.gpsimd, WA[:, i], compact, GRP * (RING * it + i), wa_ready)

            def s2_weights(k):
                turn = 0
                for end, matrices in zip(PROD_TURNS, (layer1_matrices, layer0_matrices)):
                    phase(RS[:, 1], before_s2(k), turn, end, r_done, before_r(0))
                    matrices(k)
                    turn = end
                phase(RS[:, 1], before_s2(k), turn, GROUPS // RING, r_done, before_r(0))

            def t1_weights(k):
                phase(RT[:, 0], before_t1(k), 0, GROUPS // RING, rt_ready, rt_there(k - 1))

            s2_weights(0)
            t1_weights(1)
            with pool.Fori(1, BLOCKS - 1) as k:
                s2_weights(k)
                t1_weights(k + 1)
            s2_weights(BLOCKS - 1)
            pool.wait_ge(rt_ready, rt_there(BLOCKS - 1, 1))
            for n, g in enumerate(POOL_T2):
                if n < RING:
                    pool.wait_ge(a_full, before_t1(BLOCKS) + n - RING + 1)
                else:
                    pool.wait_ge(b_full, before_t2(BLOCKS - 1) + POOL_T2[n - RING] + 1)
                spread(nc.gpsimd, WA[:, n % RING], RT[:, 1],
                       CHUNK * t2_chunk_at(g // RING) + GRP * (g % RING), wa_ready)

        @block.scalar
        def _(act):
            act.wait_ge(consts_ready, 2)
            nc.scalar.activation(warm[:, :], mask[:, 0:1], ACT.Copy).then_inc(act_step, 1)

            def copy_compact(dst, before):
                for i in range(TBANKS):
                    act.wait_ge(r_full, before + i + 1)
                    nc.scalar.activation(dst.rearrange("p t n -> p n t")[:, GRP * i:GRP * (i + 1), :],
                                         PB[i][:, :, :], ACT.Copy).then_inc(r_done, 1)

            def t1_copies(k):
                def copy(i, j):
                    act.wait_ge(a_full, before_t1(k) + RING * j + i + 1)
                    at = chunk_at(k, 0) if isinstance(j, int) and j == 0 else CHUNK * j
                    nc.scalar.activation(rows(Y, at + GRP * i), PA[i][:, :, :], ACT.Copy).then_inc(a_done, 1)

                for i in range(RING):
                    copy(i, 0)
                if first(k):
                    for j in range(1, CHUNKS):
                        if j in RS_CHUNKS:
                            copy_compact(RS[:, RS_CHUNKS.index(j), :, :], TBANKS * (1 + RS_CHUNKS.index(j)))
                        for i in range(RING):
                            copy(i, j)
                else:
                    with act.Fori(1, CHUNKS) as j:
                        for i in range(RING):
                            copy(i, j)

            copy_compact(RT[:, 0, :, :], 0)
            t1_copies(0)

            def s_phase(k):
                def copy(i, g):
                    act.wait_ge(a_full, before_s2(k) + g + 1)
                    nc.scalar.activation(columns(X, k, GRP * g), PA[i][:, :, :], ACT.Copy).then_inc(a_done, 1)

                with act.Fori(0, R_TURN - 1) as it:
                    for i in range(RING):
                        copy(i, RING * it + i)
                for i in range(RING):
                    if RING * (R_TURN - 1) + i == R_GROUP - 1:
                        act.wait_ge(r_full, before_r(k) + 1)
                        nc.scalar.activation(RC.rearrange("q l h t -> q (l h) t"), PA[R_BANK][:, :, :], ACT.Copy
                                             ).then_inc(r_done, 1)
                    copy(i, RING * (R_TURN - 1) + i)
                with act.Fori(R_TURN, GROUPS // RING - LAYERS) as it:
                    for i in range(RING):
                        copy(i, RING * it + i)
                act.wait_ge(rn_loaded, DMA * RN_DMAS * (k + 1))
                parts = [(l, RT_ROWS * i) for l in (1, 0) for i in range(RING)]
                for n in range(len(parts)):
                    for l, t in parts[min(2 * n, n + 2):min(2 * n + 2, n + 3)]:
                        rn = RN[:, CH * ROWS * l:CH * ROWS * (l + 1)].rearrange("p (n t) -> p t n", n=CH)
                        nc.scalar.activation(RT[:, l, t:t + RT_ROWS, :], rn[:, t:t + RT_ROWS, :], ACT.Copy
                                             ).then_inc(rt_ready, 1)
                    copy(n % RING, GROUPS - len(parts) + n)

            def block_steps(k):
                s_phase(k)
                t1_copies(k + 1)

            block_steps(0)
            with act.Fori(1, BLOCKS - 1) as k:
                block_steps(k)
            s_phase(BLOCKS - 1)

        @block.vector
        def _(dve):
            step = [0]

            def chained(instruction):
                step[0] += 1
                instruction.then_inc(dve_step, 1)
                dve.wait_ge(dve_step, step[0])

            def row_matrices():
                shape = [P, CH, CH]
                q1, q2 = ([QP[:, 0, (RANK * j + i) * CH:(RANK * j + i + 1) * CH] for i in range(RANK)]
                          for j in range(2))
                prod = PROD[0]
                for i in range(RANK):
                    chained(nc.vector.tensor_tensor(prod[:, i], q1[i].unsqueeze(2).broadcast_to(shape),
                                                    q2[i].unsqueeze(1).broadcast_to(shape), ALU.mult))
                diagonal = prod[:, 0].rearrange("t c n -> t (c n)")[:, 0:CH * CH:CH + 1]
                chained(nc.vector.tensor_tensor(diagonal, diagonal, QP[:, 0, 2 * RANK * CH:PARAMS], ALU.add))
                for i in range(TBANKS):
                    terms = [prod[:, r, :, GRP * i:GRP * (i + 1)].unsqueeze(1).broadcast_to(
                        [P, SPLIT, CH, GRP]) for r in range(RANK)]
                    nc.vector.tensor_tensor(AT[:, :, :, GRP * i:GRP * (i + 1)], terms[0], terms[1], ALU.add
                                            ).then_inc(at_ready, 1)

            def t1_weights(j):
                if j >= B_SLOTS:
                    dve.wait_ge(a_full, RING * (j - B_SLOTS) + 1)
                spread(nc.vector, WB[:, j % B_SLOTS], RT[:, 0], CHUNK * j, wb_ready)

            def column_matrices(l, chunks):
                shape = [P, SPLIT, CH, CH]
                kw = [[KP[l][:, :, (RANK * j + i) * CH:(RANK * j + i + 1) * CH] for i in range(RANK)]
                      for j in range(2)]
                dd = KP[l][:, :, 2 * RANK * CH:PARAMS]
                dve.wait_ge(k_loaded[l], DMA * 4)
                for i in range(RANK):
                    chained(nc.vector.tensor_tensor((AS[l], ASTMP)[i], kw[0][i].unsqueeze(3).broadcast_to(shape),
                                                    kw[1][i].unsqueeze(2).broadcast_to(shape), ALU.mult))
                    t1_weights(chunks[i])
                chained(nc.vector.tensor_tensor(AS[l], AS[l], ASTMP, ALU.add))
                t1_weights(chunks[RANK])
                diagonal = AS[l].rearrange("s p c n -> s p (c n)")[:, :, 0:CH * CH:CH + 1]
                chained(nc.vector.tensor_tensor(diagonal, diagonal, dd, ALU.add))
                wi = WI[l].rearrange("s c n -> s (c n)")
                chained(nc.vector.tensor_scalar(wi[:, 0:CH * CH:CH + 1], wi[:, 0:CH * CH:CH + 1], 1.0, None,
                                                ALU.add))
                nc.vector.tensor_tensor(AS[l], AS[l], WI[l].unsqueeze(1).broadcast_to(shape), ALU.add
                                        ).then_inc(as_ready, 1)

            def add_columns(i, k, g):
                at = columns(Y, k, GRP * g)
                nc.vector.tensor_tensor(at, PB[i][:, :, :], at, ALU.add).then_inc(b_done, 1)

            def add_rows(i, k, o):
                nc.vector.tensor_tensor(OUT[:, o % SLOTS, GRP * i:GRP * (i + 1), :], PB[i][:, :, :],
                                        rows(X, chunk_at(k, t2_chunk_at(o)) + GRP * i), ALU.add).then_inc(b_done, 1)

            def s1_weights(i, g):
                spread(nc.vector, WB[:, i % B_SLOTS], RS[:, 0], GRP * g, wb_ready)

            def t2_weights(slot, g):
                row = CHUNK * t2_chunk_at(g // RING) + GRP * (g % RING)
                spread(nc.vector, WB[:, slot], RT[:, 1], row, wb_ready)

            def s_phase(k):
                with dve.Fori(0, GROUPS // RING - 1) as it:
                    for i in range(RING):
                        dve.wait_ge(b_full, before_s1(k) + RING * it + i + 1)
                        s1_weights(i, RING * it + i + B_SLOTS)
                        if i == 0:
                            dve.wait_ge(a_done, before_s2(k))
                        add_columns(i, k, RING * it + i)
                for i in range(RING):
                    g = GROUPS - RING + i
                    dve.wait_ge(b_full, before_s1(k) + g + 1)
                    if g + B_SLOTS < GROUPS:
                        s1_weights(i, g + B_SLOTS)
                    else:
                        if g + B_SLOTS == GROUPS:
                            dve.wait_ge(rt_ready, rt_there(k, 1))
                        t2_weights(i % B_SLOTS, g + B_SLOTS - GROUPS)
                    add_columns(i, k, g)

            def t_phase(k, last):
                for g in range(GROUPS):
                    i, o = g % RING, g // RING
                    dve.wait_ge(b_full, before_t2(k) + g + 1)
                    if last:
                        n = DVE_T2.index(g) + B_SLOTS if g in DVE_T2 else len(DVE_T2)
                        if n < len(DVE_T2):
                            t2_weights(n % B_SLOTS, DVE_T2[n])
                    elif g + B_SLOTS < GROUPS:
                        t2_weights(i % B_SLOTS, g + B_SLOTS)
                    else:
                        s1_weights(i, g + B_SLOTS - GROUPS)
                    if g == 0:
                        dve.wait_ge(a_done, before_t1(k + 1))
                        dve.wait_ge(rt_ready, rt_there(k))
                    if i == 0:
                        for semaphore, done in stores_of(k, o, [o % SLOTS]):
                            dve.wait_ge(semaphore, done)
                    add_rows(i, k, o)

            dve.wait_ge(q_loaded, DMA * 3)
            row_matrices()
            dve.wait_ge(consts_ready, 2)
            dve.wait_ge(r_done, TBANKS)
            t1_weights(0)
            dve.wait_ge(at_ready, TBANKS)
            column_matrices(0, (1, 2, 3))
            dve.wait_ge(as_ready, 1)
            column_matrices(1, (4, 5, 6))
            t1_weights(CHUNKS - 1)
            dve.wait_ge(r_done, 2 * TBANKS)
            dve.wait_ge(a_full, RING * (CHUNKS - 1) + 1)
            for i in range(B_SLOTS):
                s1_weights(i, i)
            s_phase(0)
            t_phase(0, False)
            with dve.Fori(1, BLOCKS - 1) as k:
                s_phase(k)
                t_phase(k, False)
            s_phase(BLOCKS - 1)
            t_phase(BLOCKS - 1, True)

        @block.tensor
        def _(pe):
            def transpose_bank(src, i):
                by_n = src.rearrange("t p c n -> t (p c) n")
                for j in range(GRP):
                    last = nc.tensor.transpose(PB[i][:, j, :], by_n[:, :, GRP * i + j], ident[:, :])
                last.then_inc(r_full, 1)

            def multiply(bank, weights, moving, full):
                for j in range(GRP):
                    last = nc.tensor.matmul(bank[:, j, :], weights[:, j].rearrange("p q n -> p (q n)"), moving(j),
                                            start=True, stop=True)
                last.then_inc(full, 1)

            def row(buf, t):
                return buf[:, bass.ds(t, 1), :].rearrange("p t s -> p (t s)")

            def column(buf, k, s):
                return buf[:, bass.ds(place(k)[0], ROWS), bass.ds(s, 1)].rearrange("p t s -> p (t s)")

            def t1(i, k, j):
                if i == 0:
                    pe.wait_ge(x_loaded[j], DMA * SPLIT * (k + 1))
                g = RING * j + i
                weights = WA[:, i]
                if not first(k):
                    pe.wait_ge(wa_ready, wa_count(before_t1(k)) + g + 1)
                elif i == 0:
                    pe.wait_ge(wb_ready, j + 1)
                    weights = WB[:, j % B_SLOTS]
                else:
                    pe.wait_ge(wa_ready, (RING - 1) * j + i)
                if g >= RING or not first(k):
                    pe.wait_ge(a_done, before_t1(k) + g - RING + 1)
                multiply(PA[i], weights, lambda r: row(X, chunk_at(k, j) + GRP * i + r), a_full)

            def s2(i, k, g):
                pe.wait_ge(wa_ready, wa_count(before_s2(k)) + g + 1)
                pe.wait_ge(a_done, before_s2(k) + g - RING + 1)
                pe.wait_ge(b_done, before_s1(k) + g + 1)
                multiply(PA[i], WA[:, i], lambda r: column(Y, k, GRP * g + r), a_full)

            def s1(i, k, g):
                pe.wait_ge(wb_ready, wb_count(before_s1(k)) + g + 1)
                if not (first(k) and isinstance(g, int) and g < RING):
                    pe.wait_ge(b_done, before_s1(k) + g - RING + 1)
                multiply(PB[i], WB[:, i % B_SLOTS], lambda r: column(X, k, GRP * g + r), b_full)

            def t2(k, g, last):
                i, o = g % RING, g // RING
                if not last:
                    pe.wait_ge(wb_ready, wb_count(before_t2(k)) + g + 1)
                    weights = WB[:, i % B_SLOTS]
                elif g in DVE_T2:
                    n = DVE_T2.index(g)
                    pe.wait_ge(wb_ready, wb_count(before_t2(k)) + n + 1)
                    weights = WB[:, n % B_SLOTS]
                else:
                    n = POOL_T2.index(g)
                    pe.wait_ge(wa_ready, wa_count(before_t1(k + 1)) + n + 1)
                    weights = WA[:, n % RING]
                pe.wait_ge(b_done, before_t2(k) + max(0, g - RING + 1))
                multiply(PB[i], weights, lambda r: row(Y, chunk_at(k, t2_chunk_at(o)) + GRP * i + r), b_full)

            def s_phase(k, last):
                for g in range(1, RING):
                    s1(g, k, g)
                    if g >= LAG:
                        s2(g - LAG, k, g - LAG)

                def turns(start, end):
                    with pe.Fori(start, end) as it:
                        for i in range(RING):
                            s1(i, k, RING * it + i)
                            s2((i - LAG) % RING, k, RING * it + i - LAG)

                turns(1, R_TURN)
                pe.wait_ge(prod_ready, LAYERS * (k + 1))
                pe.wait_ge(a_done, before_s2(k) + R_GROUP - RING + 1)
                for l in range(LAYERS):
                    for h in range(HALVES):
                        by_cn = PROD[l][:, 0].rearrange("t c n -> t (c n)")
                        last_one = nc.tensor.transpose(PA[R_BANK][:, HALVES * l + h, :],
                                                       by_cn[:, P * h:P * (h + 1)], ident[:, :])
                last_one.then_inc(r_full, 1)
                for i in range(RING):
                    s1(i, k, RING * R_TURN + i)
                    if RING * R_TURN + i - LAG == R_GROUP:
                        pe.wait_ge(r_done, before_r(k) + 1)
                    s2((i - LAG) % RING, k, RING * R_TURN + i - LAG)
                turns(R_TURN + 1, GROUPS // RING)
                for i in range(LAG):
                    g = GROUPS - LAG + i
                    s2(g % RING, k, g)
                    if g >= GROUPS - EARLY:
                        t2(k, g - GROUPS + EARLY, last)

            pe.wait_ge(consts_ready, 1)
            for i in range(TBANKS):
                pe.wait_ge(at_ready, i + 1)
                transpose_bank(AT, i)
            for j in range(CHUNKS):
                if j in RS_CHUNKS:
                    l = RS_CHUNKS.index(j)
                    pe.wait_ge(as_ready, l + 1)
                    pe.wait_ge(r_done, TBANKS * (1 + l))
                    for i in range(TBANKS):
                        transpose_bank(AS[l], i)
                for i in range(RING):
                    t1(i, 0, j)

            def block_steps(k):
                s_phase(k, False)
                done = EARLY
                for g in range(GROUPS):
                    while done < t2_before_t1(g):
                        t2(k, done, False)
                        done += 1
                    if g == GROUPS - 1:
                        s1(0, k + 1, 0)
                    t1(g % RING, k + 1, g // RING)

            pe.wait_ge(r_done, before_r(0))
            s1(0, 0, 0)
            block_steps(0)
            with pe.Fori(1, BLOCKS - 1) as k:
                block_steps(k)
            s_phase(BLOCKS - 1, True)
            for g in range(EARLY, GROUPS):
                t2(BLOCKS - 1, g, True)


_LAYER_INPUTS = ['w', 'qw1', 'qw2', 'qdd', 'kw1', 'kw2', 'kdd']


def kernel(**inputs):
    import numpy as _np
    import concourse.bacc as _bacc
    from concourse import mybir as _mybir
    from concourse.bass_utils import run_bass_kernel_spmd as _run

    nc = _bacc.Bacc("TRN2", target_bir_lowering=False, num_devices=1, dynamic_dma_scratch_size=1024)
    arrays, aps = {}, {}
    for name in ['x'] + [f"L{l}_conv_{n}" for l in range(2) for n in _LAYER_INPUTS]:
        a = _np.ascontiguousarray(inputs[name])
        a = a.reshape(a.shape[1:]) if name == 'x' or name.endswith('_w') else a.reshape(a.shape[1], -1)
        arrays[f"in_{name}_dram"] = a
        aps[name] = nc.dram_tensor(f"in_{name}_dram", a.shape, _mybir.dt.from_np(a.dtype),
                                   kind="ExternalInput").ap()
    out = nc.dram_tensor("out_0_dram", (1,) + tuple(arrays["in_x_dram"].shape), _mybir.dt.float32,
                         kind="ExternalOutput").ap()
    cross_conv_kernel(
        nc, aps['x'],
        [tuple(aps[f"L{l}_conv_{n}"] for n in ('qw1', 'qw2', 'qdd')) for l in range(2)],
        [tuple(aps[f"L{l}_conv_{n}"] for n in ('kw1', 'kw2', 'kdd')) for l in range(2)],
        [aps[f"L{l}_conv_w"] for l in range(2)],
        out[0])
    r = _run(nc, [arrays], core_ids=[0])
    return r.results[0]["out_0_dram"]
```
